# Optimizing a Trainium2 kernel written in Bass

```python
import numpy as np
import jax
import jax.numpy as jnp

def _softmax(x, axis=-1):
    return jax.nn.softmax(x, axis=axis)

def _gelu(x):
    return jax.nn.gelu(x, approximate=True)

def _silu(x):
    return jax.nn.silu(x)

def _sigmoid(x):
    return jax.nn.sigmoid(x)

def _layernorm(x, axis=-1, eps=1e-05):
    m = jnp.mean(x, axis=axis, keepdims=True)
    v = jnp.var(x, axis=axis, keepdims=True)
    return (x - m) / jnp.sqrt(v + eps)

def _scatter_add(tgt, idx, src, axis=0):
    return tgt.at[idx].add(src)

def _segment_sum(src, seg, n):
    return jax.ops.segment_sum(src, seg, n)
kernel_name = 'mk_rec_standalone_d1_rec_r8_8bbeec'

def setup_inputs(seed: int=0):
    np.random.seed(seed)
    _w = jnp.asarray

    def _rec_inputs():
        import jax
        import jax.numpy as jnp
        _rk = jax.random.key(seed)
        r_numerical = 8.7408e-05 + 1.0001 * jax.random.normal(jax.random.fold_in(_rk, 1), (2048, 13), jnp.float32)
        r_cat_features = jnp.stack([jax.random.randint(jax.random.fold_in(jax.random.fold_in(_rk, 2), 0), (2048,), 2, 12500, jnp.int32), jax.random.randint(jax.random.fold_in(jax.random.fold_in(_rk, 2), 1), (2048,), 1, 99999, jnp.int32), jax.random.randint(jax.random.fold_in(jax.random.fold_in(_rk, 2), 2), (2048,), 0, 12500, jnp.int32), jax.random.randint(jax.random.fold_in(jax.random.fold_in(_rk, 2), 3), (2048,), 0, 12500, jnp.int32), jax.random.randint(jax.random.fold_in(jax.random.fold_in(_rk, 2), 4), (2048,), 10, 99997, jnp.int32), jax.random.randint(jax.random.fold_in(jax.random.fold_in(_rk, 2), 5), (2048,), 0, 99993, jnp.int32), jax.random.randint(jax.random.fold_in(jax.random.fold_in(_rk, 2), 6), (2048,), 2, 99999, jnp.int32), jax.random.randint(jax.random.fold_in(jax.random.fold_in(_rk, 2), 7), (2048,), 1, 99995, jnp.int32), jax.random.randint(jax.random.fold_in(jax.random.fold_in(_rk, 2), 8), (2048,), 0, 12500, jnp.int32), jax.random.randint(jax.random.fold_in(jax.random.fold_in(_rk, 2), 9), (2048,), 2, 99999, jnp.int32), jax.random.randint(jax.random.fold_in(jax.random.fold_in(_rk, 2), 10), (2048,), 0, 99999, jnp.int32), jax.random.randint(jax.random.fold_in(jax.random.fold_in(_rk, 2), 11), (2048,), 6, 99999, jnp.int32), jax.random.randint(jax.random.fold_in(jax.random.fold_in(_rk, 2), 12), (2048,), 0, 99999, jnp.int32), jax.random.randint(jax.random.fold_in(jax.random.fold_in(_rk, 2), 13), (2048,), 3, 99996, jnp.int32), jax.random.randint(jax.random.fold_in(jax.random.fold_in(_rk, 2), 14), (2048,), 0, 99999, jnp.int32), jax.random.randint(jax.random.fold_in(jax.random.fold_in(_rk, 2), 15), (2048,), 3, 99997, jnp.int32), jax.random.randint(jax.random.fold_in(jax.random.fold_in(_rk, 2), 16), (2048,), 0, 99999, jnp.int32), jax.random.randint(jax.random.fold_in(jax.random.fold_in(_rk, 2), 17), (2048,), 0, 99998, jnp.int32), jax.random.randint(jax.random.fold_in(jax.random.fold_in(_rk, 2), 18), (2048,), 10, 99997, jnp.int32), jax.random.randint(jax.random.fold_in(jax.random.fold_in(_rk, 2), 19), (2048,), 0, 99999, jnp.int32), jax.random.randint(jax.random.fold_in(jax.random.fold_in(_rk, 2), 20), (2048,), 0, 12500, jnp.int32), jax.random.randint(jax.random.fold_in(jax.random.fold_in(_rk, 2), 21), (2048,), 1, 12500, jnp.int32), jax.random.randint(jax.random.fold_in(jax.random.fold_in(_rk, 2), 22), (2048,), 1, 99997, jnp.int32), jax.random.randint(jax.random.fold_in(jax.random.fold_in(_rk, 2), 23), (2048,), 2, 12500, jnp.int32), jax.random.randint(jax.random.fold_in(jax.random.fold_in(_rk, 2), 24), (2048,), 1, 12500, jnp.int32), jax.random.randint(jax.random.fold_in(jax.random.fold_in(_rk, 2), 25), (2048,), 2, 99995, jnp.int32)], axis=1)
        return (r_numerical, r_cat_features)
    r_numerical, r_cat_features = _rec_inputs()

    def _L0_rec_setup():
        import jax, jax.numpy as jnp
        import numpy as np
        B = 4096
        NUM_DENSE = 13
        PAD_DENSE = 16
        T = 26
        V = 12500
        E = 128
        BOTTOM_DIMS = [512, 256, 128]
        TOP_DIMS = [1024, 1024, 512, 256, 1]
        N_FEAT = T + 1
        PAIR = N_FEAT * (N_FEAT - 1) // 2
        TOP_IN = PAIR + E
        TOP_PAD = 480

        def _glorot(key, fan_in, fan_out):
            s = np.sqrt(2.0 / (fan_in + fan_out))
            return jax.random.normal(key, (fan_in, fan_out), jnp.float32) * s
        key = jax.random.key(seed)
        ks = jax.random.split(key, 32)
        inp = {'numerical': jax.random.normal(ks[0], (B, NUM_DENSE), jnp.float32), 'cat_features': jax.random.randint(ks[1], (B, T), 0, V, jnp.int32), 'emb_tables': jax.random.normal(ks[2], (T, V, E), jnp.float32) * 0.01}
        d_in = PAD_DENSE
        for i, d in enumerate(BOTTOM_DIMS):
            inp[f'bw{i}'] = _glorot(ks[3 + 2 * i], d_in, d)
            inp[f'bb{i}'] = jax.random.normal(ks[4 + 2 * i], (d,), jnp.float32) * np.sqrt(1.0 / d)
            d_in = d
        d_in = TOP_PAD
        for i, d in enumerate(TOP_DIMS):
            inp[f'tw{i}'] = _glorot(ks[12 + 2 * i], d_in, d)
            inp[f'tb{i}'] = jax.random.normal(ks[13 + 2 * i], (d,), jnp.float32) * np.sqrt(1.0 / d)
            d_in = d
        return inp
    _L0_rec_all = _L0_rec_setup()
    _L0_rec_in = {k: v for k, v in _L0_rec_all.items() if k in ('emb_tables', 'bw0', 'bb0', 'bw1', 'bb1', 'bw2', 'bb2', 'tw0', 'tb0', 'tw1', 'tb1', 'tw2', 'tb2', 'tw3', 'tb3', 'tw4', 'tb4')}
    del _L0_rec_all
    return {'r_numerical': r_numerical, 'r_cat_features': r_cat_features, 'L0_rec_emb_tables': _L0_rec_in['emb_tables'], 'L0_rec_bw0': _L0_rec_in['bw0'], 'L0_rec_bb0': _L0_rec_in['bb0'], 'L0_rec_bw1': _L0_rec_in['bw1'], 'L0_rec_bb1': _L0_rec_in['bb1'], 'L0_rec_bw2': _L0_rec_in['bw2'], 'L0_rec_bb2': _L0_rec_in['bb2'], 'L0_rec_tw0': _L0_rec_in['tw0'], 'L0_rec_tb0': _L0_rec_in['tb0'], 'L0_rec_tw1': _L0_rec_in['tw1'], 'L0_rec_tb1': _L0_rec_in['tb1'], 'L0_rec_tw2': _L0_rec_in['tw2'], 'L0_rec_tb2': _L0_rec_in['tb2'], 'L0_rec_tw3': _L0_rec_in['tw3'], 'L0_rec_tb3': _L0_rec_in['tb3'], 'L0_rec_tw4': _L0_rec_in['tw4'], 'L0_rec_tb4': _L0_rec_in['tb4']}

def reference(r_numerical, r_cat_features, L0_rec_emb_tables, L0_rec_bw0, L0_rec_bb0, L0_rec_bw1, L0_rec_bb1, L0_rec_bw2, L0_rec_bb2, L0_rec_tw0, L0_rec_tb0, L0_rec_tw1, L0_rec_tb1, L0_rec_tw2, L0_rec_tb2, L0_rec_tw3, L0_rec_tb3, L0_rec_tw4, L0_rec_tb4):
    import jax
    import jax.numpy as jnp

    def _L0_rec_ref(numerical, cat_features, emb_tables, bw0, bb0, bw1, bb1, bw2, bb2, tw0, tb0, tw1, tb1, tw2, tb2, tw3, tb3, tw4, tb4):
        import jax, jax.numpy as jnp
        import numpy as np
        B = 4096
        NUM_DENSE = 13
        PAD_DENSE = 16
        T = 26
        V = 12500
        E = 128
        BOTTOM_DIMS = [512, 256, 128]
        TOP_DIMS = [1024, 1024, 512, 256, 1]
        N_FEAT = T + 1
        PAIR = N_FEAT * (N_FEAT - 1) // 2
        TOP_IN = PAIR + E
        TOP_PAD = 480

        def _glorot(key, fan_in, fan_out):
            s = np.sqrt(2.0 / (fan_in + fan_out))
            return jax.random.normal(key, (fan_in, fan_out), jnp.float32) * s
        b = numerical.shape[0]
        x = jnp.pad(numerical, ((0, 0), (0, PAD_DENSE - NUM_DENSE)))
        for w, bias in ((bw0, bb0), (bw1, bb1), (bw2, bb2)):
            x = jax.nn.relu(x @ w + bias)
        bottom_out = x
        emb_out = jax.vmap(lambda tab, idx: tab[idx], in_axes=(0, 1), out_axes=1)(emb_tables, cat_features)
        feats = jnp.concatenate([bottom_out[:, None, :], emb_out], axis=1)
        Z = jnp.einsum('bnd,bmd->bnm', feats, feats)
        iu, ju = jnp.triu_indices(N_FEAT, k=1)
        pair = Z[:, iu, ju]
        x = jnp.concatenate([bottom_out, pair, jnp.zeros((b, TOP_PAD - TOP_IN), feats.dtype)], axis=1)
        tops = ((tw0, tb0), (tw1, tb1), (tw2, tb2), (tw3, tb3), (tw4, tb4))
        for i, (w, bias) in enumerate(tops):
            x = x @ w + bias
            if i < len(tops) - 1:
                x = jax.nn.relu(x)
        return x
    y = _L0_rec_ref(r_numerical, r_cat_features, L0_rec_emb_tables, L0_rec_bw0, L0_rec_bb0, L0_rec_bw1, L0_rec_bb1, L0_rec_bw2, L0_rec_bb2, L0_rec_tw0, L0_rec_tb0, L0_rec_tw1, L0_rec_tb1, L0_rec_tw2, L0_rec_tb2, L0_rec_tw3, L0_rec_tb3, L0_rec_tw4, L0_rec_tb4)
    return y

_drawn_inputs = setup_inputs


def setup_inputs(seed=0):
    import zlib

    import numpy as np

    out = dict(_drawn_inputs(seed))
    spreads = {}
    factors = {}
    for name, (base, spread) in spreads.items():
        noise = np.random.default_rng([zlib.crc32(name.encode()), seed]).standard_normal(out[name].shape)
        drawn = base * np.exp(spread * noise) if base else spread * noise
        out[name] = jnp.asarray(drawn.astype(out[name].dtype))
    for name, factor in factors.items():
        out[name] = (out[name] * factor).astype(out[name].dtype)
    return out
```

```python
from contextlib import ExitStack

import concourse.bass as bass
from concourse import mybir

P = 128
F32 = mybir.dt.float32
F32R = mybir.dt.float32r
I32 = mybir.dt.int32
U32 = mybir.dt.uint32
ALU = mybir.AluOpType
ACT = mybir.ActivationFunctionType

CH = 256
BATCH = 64
CUTS = (0, 4, 7, 10, 13)
XPOS = 1
PACE = 0.9
XPOS = 1
PACE = 0.9
AHEAD = 8


def dlrm(nc, x, cat, emb, bw, bb, tw, tb, out):
    S, ND = x.shape
    T, V, E = emb.shape
    F = T + 1
    NCH, NB = S // CH, S // BATCH
    G = CH // 4
    GPB = BATCH * T // P
    STEPS = CH // 16
    NI = S * T // P
    IR = NI // 4
    D0, D1, D2 = (w.shape[1] for w in bw)
    H0, H1, H2, H3, _ = (w.shape[1] for w in tw)
    KX = tw[0].shape[0]
    XK = [min(P, KX - k * P) for k in range((KX + P - 1) // P)]
    assert E == P and D2 == P and GPB == CUTS[-1] and GPB * P == BATCH * T
    assert (26 * IR) % 26 == 0 and (P * IR) % T == 0

    with ExitStack() as ctx:
        def sb(name, shape, dt=F32):
            return ctx.enter_context(nc.sbuf_tensor(name, shape, dt))

        def psum(name, shape):
            return ctx.enter_context(nc.psum_tensor(name, shape, F32))

        def sem(name):
            return ctx.enter_context(nc.semaphore(name))

        unit = 512
        NU = (4 * H0 + 8 * H1 + 8 * H2 + 4 * H3) // unit
        w_hi = sb("w_hi", [P, NU * unit], F32R)
        w_lo = sb("w_lo", [P, NU * unit], F32R)
        w_last = sb("w_last", [P, 2])
        base = [0, 4 * H0, 4 * H0 + 8 * H1, 4 * H0 + 8 * H1 + 8 * H2]
        b_bot = sb("b_bot", [P, (D0 + D1 + D2) // P])
        b_top = sb("b_top", [P, (H0 + H1 + H2 + H3) // P])
        b_last = sb("b_last", [1, 1])
        ident = sb("ident", [P, P])
        idx = sb("idx", [P, NI], I32)
        idx_now = sb("idx_now", [P, 2, GPB], I32)
        offs = sb("offs", [P, GPB])
        offs_t = sb("offs_t", [P, GPB])
        bottom = sb("bottom", [P, S])
        rows = sb("rows", [P, GPB, E])
        feat = sb("feat", [P, BATCH, 32])
        gram = sb("gram", [P, F, G])
        xin = sb("xin", [P, 2, 4, CH], F32R)
        act_f = sb("act_f", [P, 2, CH])
        stage = sb("stage", [P, 2, unit])
        ybuf = sb("ybuf", [1, CH])
        arena = sb("arena", [P, 6144], F32R)
        h0 = arena[:, 0:4096].rearrange("p (a t n) -> p a t n", a=2, t=8)
        h1 = arena[:, 4096:6144].rearrange("p (a t n) -> p a t n", a=2, t=4)
        h2 = h0[:, :, 4:8]
        h3 = stage[:, 0, :].rearrange("p (t n) -> p t n", t=2)
        wb0 = arena[:, 0:512]
        wb1 = arena[:, 512:2560].rearrange("p (a k n) -> p a k n", a=2, k=4)
        wb2 = arena[:, 2560:3072].rearrange("p (a k n) -> p a k n", a=2, k=2)
        x1 = arena[:, 3072:5120].rearrange("p (a t n) -> p a t n", a=2, t=4)
        x2 = arena[:, 5120:6144].rearrange("p (a t n) -> p a t n", a=2, t=2)
        xT = xin[:].rearrange("p a k n -> p (a k n)")
        rows_flat = rows[:].rearrange("p i e -> p (i e)")
        cat_i = rows_flat[0:IR, 0:512].bitcast(I32)
        cat_f = rows_flat[0:IR, 512:1024]
        cat_w = rows_flat[0:IR, 1024:1536]
        gram_flat = gram[:].rearrange("p f g -> p (f g)")
        raw1 = gram_flat[:, 0:4 * D1]
        raw2 = gram_flat[:, 4 * D1:4 * D1 + 2 * D2]
        raw0 = act_f[:].rearrange("p a n -> p (a n)")
        x_raw = gram_flat[:, 1280:1280 + 16 * ND].rearrange("p (b d) -> p b d", d=ND)
        x_rep = bottom[:].rearrange("p (b q r) -> p b q r", b=16, q=4)

        Z = nc.dram_tensor("gram_scratch", (P, F, G), F32, kind="Internal").ap()
        Zv = Z.rearrange("(j m) f g -> m f j g", j=4)

        ps_t = psum("ps_t", [P, 2, 512])
        ps_g = psum("ps_g", [P, 2, 512])
        ps_m = psum("ps_m", [P, 2, 512])
        ps_a = psum("ps_a", [P, 2, 512])

        const_done = sem("const_done")
        zero_done = sem("zero_done")
        cat_in = sem("cat_in")
        x_loaded = sem("x_loaded")
        wb_in = sem("wb_in")
        bias_in = sem("bias_in")
        cat_step = sem("cat_step")
        offs_step = sem("offs_step")
        idx_turned = sem("idx_turned")
        idx_ready = sem("idx_ready")
        idx_copied = sem("idx_copied")
        steps_begun = sem("steps_begun")
        x_turned = sem("x_turned")
        xT_step = sem("xT_step")
        wb_step = sem("wb_step")
        stage_in = [sem(f"stage_in{i}") for i in range(2)]
        w_split = sem("w_split")
        w_high = sem("w_high")
        gathered = [sem(f"gathered{i}") for i in range(4)]
        rows_turned = sem("rows_turned")
        feat_ready = sem("feat_ready")
        gram_done = sem("gram_done")
        gram_out = sem("gram_out")
        z_written = sem("z_written")
        pairs_in = [sem(f"pairs_in{i}") for i in range(3)]
        x_high = sem("x_high")
        x_ready = sem("x_ready")
        bot_mm = sem("bot_mm")
        bot_ev = sem("bot_ev")
        bot_high = sem("bot_high")
        bot_split = sem("bot_split")
        mlp_mm = sem("mlp_mm")
        mlp_ev = sem("mlp_ev")
        h_high = sem("h_high")
        h_split = sem("h_split")
        l2_step = sem("l2_step")
        y_out = sem("y_out")

        PRE = 3
        OUTS = ([("L0", m) for m in range(PRE, 8)] + [("L1", m) for m in range(8)] +
                [("L2", m) for m in range(4)] + [("N0", m) for m in range(PRE)] +
                [("L3", m) for m in range(2)] + [("L4", 0)])
        NO = len(OUTS)
        SPLIT = [o for o in OUTS if o[0] in ("L0", "L1", "L2", "N0")]
        NS = len(SPLIT)
        MM = [o for o in OUTS if o[0] in ("L0", "L1", "N0", "L3")]
        NM = len(MM)
        assert NS % 2 == 0 and NM % 2 == 0

        def out_no(c, o):
            return PRE + c * NO + OUTS.index(o) + 1

        def split_no(c, o):
            return PRE + c * NS + SPLIT.index(o) + 1

        def half(o, of):
            return (PRE + of.index(o)) % 2

        def body_order():
            items = [(("L0", m), 1.28) for m in range(PRE, 8)]
            for m in range(8):
                items.append((("L1", m), 2.56))
                if m:
                    items.append((("A", m - 1), 1.28))
            items.append((("A", 7), 1.28))
            items.insert(-XPOS, (("X", 0), 0.0))
            items += [(("N0", m), 1.28) for m in range(PRE)]
            items += [(("L3", m), 1.28) for m in range(2)] + [(("L4", 0), 0.85)]
            whole = sum(t for _, t in items)
            order, at, n = [], 0.0, 0
            for o, t in items:
                while n < STEPS and at >= (n + 0.5) * PACE * whole / STEPS:
                    order.append(("prep", n))
                    n += 1
                order.append(o)
                at += t
            while n < STEPS:
                order.append(("prep", n))
                n += 1
            return order

        ORDER = body_order()
        LEFT = STEPS - AHEAD

        def body_items(last, preps):
            for o in ORDER:
                if last and o[0] in ("N0", "X"):
                    continue
                if o[0] == "prep" and o[1] > preps:
                    continue
                yield o

        READS = []
        row = 0
        for m in range(T):
            f = m + 1
            while f < F:
                k, p0 = divmod(row, P)
                take = min(F - f, P - p0)
                READS.append((k, p0, take, m, f))
                f += take
                row += take
        assert D2 + row + 1 == KX
        reads = [sum(r[0] == k for r in READS) for k in range(3)]


        block = ctx.enter_context(nc.Block())

        def jg(ap):
            return ap.rearrange("p (g j) -> p j g", j=4)

        @block.sync
        def _(sp):
            sp.dma_start(cat_i, cat.rearrange("s t -> (s t)").rearrange("(b a q) -> a b q", a=IR, q=P))\
                .then_inc(cat_in, 16)
            sp.wait_ge(zero_done, 1)
            sp.dma_start(x_raw, x.rearrange("(p b) d -> p b d", b=16)).then_inc(x_loaded, 16)
            for q in range(4):
                sp.dma_start(raw0[32 * q:32 * q + 16, :], bw[0]).then_inc(wb_in, 16)
            sp.dma_start(raw1.rearrange("p (k n) -> p k n", k=4), bw[1].rearrange("(k p) n -> p k n", p=P))\
                .then_inc(wb_in, 16)
            sp.dma_start(raw2.rearrange("p (k n) -> p k n", k=2), bw[2].rearrange("(k p) n -> p k n", p=P))\
                .then_inc(wb_in, 16)
            ctx.enter_context(nc.allow_non_contiguous_dma(reason="biases and last weights, once"))
            col = 0
            for b in bb:
                n = b.shape[0] // P
                sp.dma_start(b_bot[:, col:col + n], b.rearrange("(k p) -> p k", p=P)).then_inc(bias_in, 16)
                col += n
            col = 0
            for b in tb[:4]:
                n = b.shape[0] // P
                sp.dma_start(b_top[:, col:col + n], b.rearrange("(k p) -> p k", p=P)).then_inc(bias_in, 16)
                col += n
            sp.dma_start(b_last[:], tb[4].rearrange("(a b) -> a b", a=1)).then_inc(bias_in, 16)
            sp.dma_start(w_last[:], tw[4].rearrange("(k p) n -> p (k n)", p=P)).then_inc(bias_in, 16)

            u = 0
            for w in tw[:4]:
                K, N = w.shape
                per = min(N, unit)
                step = unit // per
                for k in range(0, (K + P - 1) // P, step):
                    for n in range(0, N, per):
                        if u >= 2:
                            sp.wait_ge(w_split, u - 1)
                        rows_here = min(P, K - k * P)
                        src = w[k * P:k * P + step * rows_here, n:n + per].rearrange("(k p) n -> p k n", k=step)
                        dst = stage[0:rows_here, u % 2, :].rearrange("p (k n) -> p k n", k=step)
                        sp.dma_start(dst, src).then_inc(stage_in[u % 2], 16)
                        u += 1
            assert u == NU

            def relayout(c, first=False):
                sp.wait_ge(gram_out, (c + 1) * STEPS)
                if not first:
                    for k in range(3):
                        sp.wait_ge(pairs_in[k], c * reads[k] * 16)
                sp.dma_start(Z, gram[:]).then_inc(z_written, 16)
                if first:
                    sp.wait_ge(bot_mm, 7 * NCH)
                else:
                    sp.wait_ge(mlp_mm, out_no(c - 1, ("L0", 7)))
                sp.wait_ge(z_written, (c + 1) * 16)
                for k, p0, n, m, f in READS:
                    dst = xin[p0:p0 + n, 1, 1 + k, :].bitcast(F32).rearrange("p (j g) -> p j g", j=4)
                    sp.dma_start(dst, Zv[m, f:f + n]).then_inc(pairs_in[k], 16)

            relayout(0, True)
            with sp.Fori(0, NCH - 1) as c:
                relayout(c + 1)
            sp.wait_ge(y_out, NCH * 16 + 16)

        @block.gpsimd
        def _(pool):
            nc.gpsimd.memset(raw0, 0.0).then_inc(zero_done, 1)
            nc.gpsimd.iota(idx_now[:, 0, :], [[-2, GPB]], base=T, channel_multiplier=1).then_inc(const_done, 1)
            nc.gpsimd.memset(ident[:], 0.0).then_inc(zero_done, 1)
            pool.wait_ge(zero_done, 2)
            nc.gpsimd.affine_select(out=ident[:], in_=ident[:], compare_op=ALU.not_equal, fill=1.0, base=0,
                                    pattern=[[-1, P]], channel_multiplier=1).then_inc(const_done, 1)
            nc.gpsimd.memset(feat[:, :, F:], 0.0).then_inc(zero_done, 1)
            table = emb.rearrange("t v e -> (t v) e")
            pool.wait_ge(idx_ready, 1)

            def batch(b, side, first=False):
                nc.gpsimd.tensor_copy(idx_now[:, side, :], idx[:, bass.ds(b * GPB, GPB)]).then_inc(idx_copied, 1)
                pool.wait_ge(idx_copied, b + 1)
                for k in range(4):
                    if not first:
                        pool.wait_ge(rows_turned, (b - 1) * 4 + k + 1)
                    pool.sem_inc(steps_begun, 1)
                    for i in range(CUTS[k], CUTS[k + 1]):
                        nc.gpsimd.indirect_dma_start(
                            rows[:, i, :], None, table,
                            bass.IndirectOffsetOnAxis(ap=idx_now[:, side, i:i + 1].bitcast(U32), axis=0),
                        ).then_inc(gathered[k], 16)

            batch(0, 0, True)
            batch(1, 1)
            with pool.Fori(1, NB // 2) as i:
                batch(i * 2, 0)
                batch(i * 2 + 1, 1)

        @block.scalar
        def _(act):
            def gram_quad(n, col, side):
                act.wait_ge(gram_done, n + 1)
                src = ps_g[:, side, 0:16 * F].rearrange("p (g j f) -> p j f g", g=4, j=4)
                for j in range(4):
                    a = 32 * j
                    last = nc.scalar.copy(gram[a:a + 32, :, bass.ds(col, 4)], src[a:a + 32, j])
                last.then_inc(gram_out, 1)

            act.wait_ge(bias_in, 9 * 16)
            act.sem_inc(y_out, 16)

            def bottom_chunk(c, first=False):
                for i in range(7):
                    act.wait_ge(bot_mm, c * 7 + i + 1)
                    if i < 6:
                        if not (first and i < 2):
                            act.wait_ge(bot_split, c * 6 + max(i - 1, 0))
                        nc.scalar.activation(act_f[:, i % 2, :], ps_m[:, i % 2, 0:CH], ACT.Relu,
                                             bias=b_bot[:, i:i + 1]).then_inc(bot_ev, 1)
                    else:
                        nc.scalar.activation(bottom[:, bass.ds(c * CH, CH)], ps_a[:, 0, 0:CH], ACT.Relu,
                                             bias=b_bot[:, i:i + 1]).then_inc(bot_ev, 1)

            def lead(i, first=False):
                bottom_chunk(i * 2, first)
                gram_quad(i * 4, i * 16, 0)
                bottom_chunk(i * 2 + 1)
                for k in range(1, 4):
                    gram_quad(i * 4 + k, i * 16 + 4 * k, k % 2)
            lead(0, True)
            with act.Fori(1, 4) as i:
                lead(i)
            act.wait_ge(z_written, 16)
            for n in range(STEPS, STEPS + AHEAD - 1):
                gram_quad(n, 4 * (n % STEPS), n % 2)

            def to_split(o, c, src, bias, no=None):
                if no is None:
                    act.wait_ge(h_split, split_no(c, o) - 2)
                    slot = half(o, SPLIT)
                else:
                    if no >= 2:
                        act.wait_ge(h_split, no - 1)
                    slot = no % 2
                nc.scalar.activation(act_f[:, slot, :], src, ACT.Relu, bias=b_top[:, bias:bias + 1])\
                    .then_inc(mlp_ev, 1)

            for m in range(PRE):
                act.wait_ge(mlp_mm, m + 1)
                to_split(None, 0, ps_m[:, m % 2, 0:CH], m, m)

            def body(c, last, preps):
                for o in body_items(last, preps):
                    kind, m = o
                    if kind == "prep":
                        q = (AHEAD + m - 1) % STEPS
                        if q == 0:
                            act.wait_ge(z_written, (c + 2) * 16)
                        gram_quad((c + 1) * STEPS + AHEAD + m - 1, 4 * q, q % 2)
                    elif kind in ("L0", "N0", "L1"):
                        act.wait_ge(mlp_mm, out_no(c, o))
                        to_split(o, c, ps_m[:, half(o, MM), 0:CH], m + (8 if kind == "L1" else 0))
                    elif o == ("A", 7):
                        for t in range(4):
                            act.wait_ge(mlp_mm, out_no(c, ("L2", t | 1)))
                            to_split(("L2", t), c, ps_a[:, t // 2, (t % 2) * CH:(t % 2 + 1) * CH], 16 + t)
                    elif kind == "L3":
                        act.wait_ge(mlp_mm, out_no(c, o) - 3 * last)
                        nc.scalar.activation(h3[:, m, :], ps_m[:, half(o, MM) ^ last, 0:CH], ACT.Relu,
                                             bias=b_top[:, 20 + m:21 + m]).then_inc(mlp_ev, 1)
                    elif kind == "L4":
                        act.wait_ge(mlp_mm, out_no(c, o) - 3 * last)
                        act.wait_ge(y_out, c * 16 + 16)
                        nc.scalar.activation(ybuf[0:1, :].rearrange("p (g j) -> p j g", j=4),
                                             ps_a[0:1, 0, 0:CH].rearrange("p (j g) -> p j g", j=4),
                                             ACT.Identity, bias=b_last[0:1, 0:1]).then_inc(mlp_ev, 1)
                        act.wait_ge(mlp_ev, out_no(c, o) - 3 * last)
                        act.dma_start(out[bass.ds(c * CH, CH), :].rearrange("s o -> o s"), ybuf[0:1, :])\
                            .then_inc(y_out, 16)

            with act.Fori(0, NCH - 2) as c:
                body(c, 0, STEPS)
            body(NCH - 2, 0, LEFT)
            body(NCH - 1, 1, -1)

        @block.vector
        def _(dve):
            dve.wait_ge(const_done, 1)
            nc.vector.tensor_copy(offs[:], idx_now[:, 0, :]).then_inc(offs_step, 1)
            step = 1
            for t in (4 * T, 2 * T, T):
                dve.wait_ge(offs_step, step)
                nc.vector.tensor_scalar(offs_t[:], offs[:], float(t), -float(t), ALU.is_ge, ALU.mult)\
                    .then_inc(offs_step, 1)
                dve.wait_ge(offs_step, step + 1)
                nc.vector.tensor_tensor(offs[:], offs[:], offs_t[:], ALU.add).then_inc(offs_step, 1)
                step += 2
            dve.wait_ge(offs_step, step)
            nc.vector.tensor_scalar(offs[:], offs[:], float(V), None, ALU.mult).then_inc(offs_step, 1)
            dve.wait_ge(cat_in, 16)
            nc.vector.tensor_scalar(cat_w, cat_i, 0.0, float(V), ALU.is_lt, ALU.mult).then_inc(cat_step, 1)
            dve.wait_ge(cat_step, 1)
            nc.vector.tensor_tensor(cat_f, cat_i, cat_w, ALU.add).then_inc(cat_step, 1)
            dve.wait_ge(cat_step, 2)
            nc.vector.tensor_scalar(cat_f, cat_f, 0.0, float(V - 1), ALU.max, ALU.min).then_inc(cat_step, 1)
            nc.vector.memset(bottom[:], 0.0).then_inc(xT_step, 1)
            dve.wait_ge(idx_turned, 1)
            dve.wait_ge(offs_step, step + 1)
            nc.vector.tensor_tensor(idx[:].rearrange("p (c k) -> p c k", k=GPB),
                                    ps_m[:, 0, 0:NI].rearrange("p (c k) -> p c k", k=GPB),
                                    offs[:].unsqueeze(1).to_broadcast([P, NI // GPB, GPB]),
                                    ALU.add).then_inc(idx_ready, 1)
            dve.wait_ge(x_loaded, 16)
            dve.wait_ge(xT_step, 1)
            for q in range(4):
                nc.vector.tensor_copy(x_rep[:, :, q, 0:ND], x_raw).then_inc(xT_step, 1)
            dve.wait_ge(wb_in, 6 * 16)
            nc.vector.tensor_copy(wb0, raw0).then_inc(wb_step, 1)
            nc.vector.tensor_copy(wb1[:, 0], raw1.rearrange("p (k n) -> p k n", k=4)).then_inc(wb_step, 1)
            nc.vector.tensor_copy(wb2[:, 0], raw2.rearrange("p (k n) -> p k n", k=2)).then_inc(wb_step, 1)
            dve.wait_ge(wb_step, 3)
            for q in (1, 3):
                a = 32 * q
                nc.vector.tensor_tensor(wb0[a:a + 32], raw0[a:a + 32], wb0[a:a + 32].bitcast(F32),
                                        ALU.subtract).then_inc(wb_step, 1)
            nc.vector.tensor_tensor(wb1[:, 1], raw1.rearrange("p (k n) -> p k n", k=4),
                                    wb1[:, 0].bitcast(F32), ALU.subtract).then_inc(wb_step, 1)
            nc.vector.tensor_tensor(wb2[:, 1], raw2.rearrange("p (k n) -> p k n", k=2),
                                    wb2[:, 0].bitcast(F32), ALU.subtract).then_inc(wb_step, 1)
            xTv = xT.rearrange("d (p b) -> d b p", b=16)
            for k in range(4):
                ps = (ps_t, ps_g)[k // 2][:, k % 2, :].rearrange("d (b p) -> d b p", b=4)
                dst = xTv[:, 4 * k:4 * k + 4, :]
                dve.wait_ge(x_turned, k + 1)
                nc.vector.tensor_copy(dst, ps).then_inc(xT_step, 1)
                dve.wait_ge(xT_step, 6 + 2 * k)
                nc.vector.tensor_tensor(dst[64:128], ps[64:128], dst[64:128].bitcast(F32), ALU.subtract)\
                    .then_inc(xT_step, 1)

            def split(high, low, src, high_done, no, done):
                nc.vector.tensor_copy(high, src).then_inc(high_done, 1)
                dve.wait_ge(high_done, no)
                nc.vector.tensor_tensor(low, src, high.bitcast(F32), ALU.subtract).then_inc(done, 1)

            def weights(u0):
                for s in range(2):
                    dve.wait_ge(stage_in[s], (u0 + 2) * 8)
                    cols = bass.ds((u0 + s) * unit, unit)
                    split(w_hi[:, cols], w_lo[:, cols], stage[:, s, :], w_high, u0 + s + 1, w_split)

            def bottom_chunk(c):
                for i in range(6):
                    dve.wait_ge(bot_ev, c * 7 + i + 1)
                    x, t = (x1, i) if i < 4 else (x2, i - 4)
                    split(x[:, 0, t, :], x[:, 1, t, :], act_f[:, i % 2, :], bot_high, c * 6 + i + 1, bot_split)

            def features(n, b, k, first=False):
                at, end = P * CUTS[k], P * CUTS[k + 1]
                if not first:
                    dve.wait_ge(gram_done, n - 2)
                s0, s1 = -(-at // T), -(-end // T)
                cols = feat[:, :, 0:F]
                nc.vector.tensor_copy(cols[:, s0:s1, 0], bottom[:, bass.ds(b * BATCH + s0, s1 - s0)])
                dve.wait_ge(rows_turned, n + 1)
                src = ps_t[:, k % 2, 0:end - at]
                last = None
                if at % T:
                    m = T - at % T
                    nc.vector.tensor_copy(cols[:, s0 - 1, F - m:F], src[:, 0:m])
                whole = end // T - s0
                m = s0 * T - at
                last = nc.vector.tensor_copy(cols[:, s0:s0 + whole, 1:F],
                                             src[:, m:m + whole * T].rearrange("p (s f) -> p s f", f=T))
                m += whole * T
                if m < end - at:
                    last = nc.vector.tensor_copy(cols[:, s1 - 1, 1:1 + end - at - m], src[:, m:end - at])
                last.then_inc(feat_ready, 1)

            def lead(i, first=False):
                bottom_chunk(i * 2)
                if first:
                    dve.wait_ge(bot_ev, 7)
                for k in range(4):
                    weights(i * 8 + 2 * k)
                    features(i * 4 + k, i, k, first)
                    if k == 1:
                        bottom_chunk(i * 2 + 1)

            lead(0, True)
            with dve.Fori(1, 4) as i:
                lead(i)
            for u in range(32, NU, 2):
                weights(u)
            dve.wait_ge(bot_ev, 7 * NCH)
            for n in range(STEPS, STEPS + AHEAD):
                features(n, n // 4, n % 4)

            def layer_input(c, first=False):
                if first:
                    dve.wait_ge(bot_mm, 7 * NCH)
                else:
                    dve.wait_ge(mlp_mm, out_no(c - 1, ("L0", 7)))
                view = lambda ap: ap.rearrange("p (j g) -> p j g", j=4)
                split(view(xin[:, 0, 0, :]), view(xin[:, 1, 0, :]),
                      bottom[:, bass.ds(c * CH, CH)].rearrange("p (g j) -> p j g", j=4),
                      x_high, c * 4 + 1, x_ready)
                for k in range(1, 4):
                    dve.wait_ge(pairs_in[k - 1], (c + 1) * (reads[k - 1] * 16))
                    rows_k = XK[k]
                    raw = xin[0:rows_k, 1, k, :]
                    nc.vector.tensor_copy(xin[0:rows_k, 0, k, :], raw.bitcast(F32)).then_inc(x_high, 1)
                    dve.wait_ge(x_high, c * 4 + k + 1)
                    nc.vector.tensor_tensor(raw, raw.bitcast(F32), xin[0:rows_k, 0, k, :].bitcast(F32),
                                            ALU.subtract).then_inc(x_ready, 1)

            def h_tile(dst, t, slot, no):
                dve.wait_ge(h_split_src[0], no[0])
                split(dst[:, 0, t, :], dst[:, 1, t, :], act_f[:, slot, :], h_high, no[1], h_split)

            h_split_src = [mlp_ev]
            layer_input(0, True)
            for m in range(PRE):
                h_tile(h0, m, m % 2, (m + 1, m + 1))

            def body(c, last, preps):
                for o in body_items(last, preps):
                    kind, m = o
                    if kind == "prep":
                        if m < preps:
                            features((c + 1) * STEPS + AHEAD + m, c * 4 + 4 + (AHEAD + m) // 4, (AHEAD + m) % 4)
                    elif kind == "X":
                        layer_input(c + 1)
                    elif kind in ("L0", "N0", "L1"):
                        h_tile(h1 if kind == "L1" else h0, m % 4 if kind == "L1" else m, half(o, SPLIT),
                               (out_no(c, o), split_no(c, o)))
                    elif o == ("A", 7):
                        for t in range(4):
                            o2 = ("L2", t)
                            h_tile(h2, t, half(o2, SPLIT), (out_no(c, o2), split_no(c, o2)))

            with dve.Fori(0, NCH - 2) as c:
                body(c, 0, STEPS)
            body(NCH - 2, 0, LEFT)
            body(NCH - 1, 1, -1)

        @block.tensor
        def _(pe):
            pe.wait_ge(const_done, 2)
            pe.wait_ge(cat_step, 3)
            for b in range(4):
                last = nc.tensor.transpose(ps_m[:, 0, b * IR:(b + 1) * IR], cat_f[:, b * P:(b + 1) * P],
                                           ident[0:IR, 0:IR])
            last.then_inc(idx_turned, 1)
            pe.wait_ge(xT_step, 5)
            for k in range(4):
                ps = (ps_t, ps_g)[k // 2]
                for b in range(4):
                    last = nc.tensor.transpose(ps[:, k % 2, b * P:(b + 1) * P],
                                               bottom[:, (4 * k + b) * P:(4 * k + b + 1) * P], ident[:])
                last.then_inc(x_turned, 1)

            def product(acc, whi, wlo, xhi, xlo, start, stop, shared=False):
                nc.tensor.matmul(acc, whi, xhi, start=start, stop=False, skip_group_check=shared)
                nc.tensor.matmul(acc, whi, xlo, start=False, stop=False, skip_group_check=shared)
                return nc.tensor.matmul(acc, wlo, xhi, start=False, stop=stop, skip_group_check=shared)

            def bottom_chunk(c):
                pe.wait_ge(bot_ev, c * 7)
                for i in range(4):
                    if i >= 2:
                        pe.wait_ge(bot_ev, c * 7 + i - 1)
                    nc.tensor.matmul(ps_m[:, i % 2, 0:CH], wb0[:, i * P:(i + 1) * P],
                                     xT[:, bass.ds(c * CH, CH)], start=True, stop=True).then_inc(bot_mm, 1)
                for i in range(4, 6):
                    pe.wait_ge(bot_ev, c * 7 + i - 1)
                    m = slice((i - 4) * P, (i - 3) * P)
                    for k in range(4):
                        if i == 4:
                            pe.wait_ge(bot_split, c * 6 + k + 1)
                        last = product(ps_m[:, i % 2, 0:CH], wb1[:, 0, k, m], wb1[:, 1, k, m],
                                       x1[:, 0, k, :], x1[:, 1, k, :], k == 0, k == 3)
                    last.then_inc(bot_mm, 1)
                for k in range(2):
                    pe.wait_ge(bot_split, c * 6 + 5 + k)
                    last = product(ps_a[:, 0, 0:CH], wb2[:, 0, k, :], wb2[:, 1, k, :],
                                   x2[:, 0, k, :], x2[:, 1, k, :], k == 0, k == 1)
                last.then_inc(bot_mm, 1)

            def turn(n, b, k, first=False):
                if not first:
                    pe.wait_ge(feat_ready, n - 1)
                pe.wait_ge(gathered[k], (b + 1) * (16 * (CUTS[k + 1] - CUTS[k])))
                for i in range(CUTS[k], CUTS[k + 1]):
                    a = P * (i - CUTS[k])
                    last = nc.tensor.transpose(ps_t[:, k % 2, a:a + P], rows[:, i, :], ident[:])
                last.then_inc(rows_turned, 1)

            def gram_products(n, k, first=False):
                pe.wait_ge(feat_ready, n + 1)
                if not first:
                    pe.wait_ge(gram_out, n - 1)
                for g in range(4):
                    four = feat[:, 16 * k + 4 * g:16 * k + 4 * g + 4, :]
                    last = nc.tensor.matmul(ps_g[:, k % 2, g * 4 * F:(g + 1) * 4 * F],
                                            four.rearrange("p s f -> p (s f)"), four[:, :, 0:F],
                                            start=True, stop=True)
                last.then_inc(gram_done, 1)

            pe.wait_ge(wb_step, 7)
            pe.wait_ge(zero_done, 3)
            pe.wait_ge(xT_step, 13)

            def lead(i, first=False):
                bottom_chunk(i * 2)
                turn(i * 4, i, 0, first)
                turn(i * 4 + 1, i, 1, first)
                gram_products(i * 4, 0, first)
                bottom_chunk(i * 2 + 1)
                turn(i * 4 + 2, i, 2)
                gram_products(i * 4 + 1, 1, first)
                turn(i * 4 + 3, i, 3)
                gram_products(i * 4 + 2, 2)
                gram_products(i * 4 + 3, 3)

            lead(0, True)
            with pe.Fori(1, 4) as i:
                lead(i)
            for n in range(STEPS, STEPS + AHEAD):
                turn(n, n // 4, n % 4)
                if n > STEPS:
                    gram_products(n - 1, (n - 1) % 4)

            def layer(acc, layer_no, N, m, tiles, x, ready=None):
                for k in range(tiles):
                    if ready is not None:
                        ready(k)
                    K = XK[k] if layer_no == 0 else P
                    cols = slice(base[layer_no] + k * N + m * P, base[layer_no] + k * N + (m + 1) * P)
                    last = product(acc, w_hi[0:K, cols], w_lo[0:K, cols], x[0:K, 0, k, :], x[0:K, 1, k, :],
                                   k == 0, k == tiles - 1)
                return last

            pe.wait_ge(w_split, NU)
            for m in range(PRE):
                if m >= 2:
                    pe.wait_ge(mlp_ev, m - 1)
                layer(ps_m[:, m % 2, 0:CH], 0, H0, m, 4, xin,
                      (lambda k: pe.wait_ge(x_ready, k + 1)) if m == 0 else None).then_inc(mlp_mm, 1)

            def body(c, last_body, preps):
                for o in body_items(last_body, preps):
                    kind, m = o
                    if kind in ("L0", "L1", "N0", "L3"):
                        j = MM.index(o) - 3 * (last_body and kind == "L3")
                        side = (PRE + j) % 2
                        acc = ps_m[:, side, 0:CH]
                        pe.wait_ge(mlp_ev, out_no(c, MM[j - 2]) if j >= 2 else out_no(c - 1, OUTS[j - 2]))
                    if kind == "prep":
                        n = (c + 1) * STEPS + AHEAD + m
                        k = (AHEAD + m) % 4
                        if m < preps:
                            turn(n, c * 4 + 4 + (AHEAD + m) // 4, k)
                        gram_products(n - 1, (k - 1) % 4)
                    elif kind == "L0":
                        layer(acc, 0, H0, m, 4, xin).then_inc(mlp_mm, 1)
                    elif kind == "N0":
                        layer(acc, 0, H0, m, 4, xin,
                              (lambda k: pe.wait_ge(x_ready, (c + 1) * 4 + k + 1)) if m == 0 else None)\
                            .then_inc(mlp_mm, 1)
                    elif kind == "L1":
                        def h0_ready(k):
                            if k == 0:
                                pe.wait_ge(h_split, split_no(c, ("L0", PRE)) - 1)
                            elif k >= PRE:
                                pe.wait_ge(h_split, split_no(c, ("L0", k)))
                        layer(acc, 1, H1, m, 8, h0, h0_ready if m == 0 else None).then_inc(mlp_mm, 1)
                    elif kind == "A":
                        if m == 0:
                            pe.wait_ge(mlp_ev, out_no(c - 1, ("L4", 0)))
                        pe.wait_ge(h_split, split_no(c, ("L1", m)))
                        for t in range(4):
                            cols = slice(base[2] + m * H2 + t * P, base[2] + m * H2 + (t + 1) * P)
                            last = product(ps_a[:, t // 2, (t % 2) * CH:(t % 2 + 1) * CH], w_hi[:, cols],
                                           w_lo[:, cols], h1[:, 0, m % 4, :], h1[:, 1, m % 4, :],
                                           m == 0 and t % 2 == 0, m == 7, shared=True)
                            if m == 7:
                                last.then_inc(mlp_mm, 1)
                    elif kind == "L3":
                        layer(acc, 3, H3, m, 4, h2,
                              (lambda k: pe.wait_ge(h_split, split_no(c, ("L2", k)))) if m == 0 else None)\
                            .then_inc(mlp_mm, 1)
                    elif kind == "L4":
                        pe.wait_ge(mlp_ev, out_no(c, ("L3", 1)) - 3 * last_body)
                        for k in range(2):
                            last = nc.tensor.matmul(ps_a[0:1, 0, 0:CH], w_last[:, k:k + 1], h3[:, k, :],
                                                    start=k == 0, stop=k == 1)
                        last.then_inc(mlp_mm, 1)

            with pe.Fori(0, NCH - 2) as c:
                body(c, 0, STEPS)
            body(NCH - 2, 0, LEFT)
            body(NCH - 1, 1, -1)


_INS = ["r_numerical", "r_cat_features", "L0_rec_emb_tables"] + \
    [f"L0_rec_b{p}{i}" for p in "wb" for i in range(3)] + [f"L0_rec_t{p}{i}" for p in "wb" for i in range(5)]


def kernel(**inputs):
    import numpy as np
    import concourse.bacc as bacc
    from concourse.bass_utils import run_bass_kernel_spmd as run

    nc = bacc.Bacc("TRN2", target_bir_lowering=False, num_devices=1)
    arrays, aps = {}, []
    for name in _INS:
        a = np.ascontiguousarray(inputs[name])
        arrays[f"in_{name}"] = a
        aps.append(nc.dram_tensor(f"in_{name}", a.shape, mybir.dt.from_np(a.dtype), kind="ExternalInput").ap())
    x, cat, emb = aps[:3]
    out = nc.dram_tensor("out_y", (x.shape[0], 1), F32, kind="ExternalOutput").ap()
    dlrm(nc, x, cat, emb, aps[3:6], aps[6:9], aps[9:14], aps[14:19], out)
    return run(nc, [arrays], core_ids=[0]).results[0]["out_y"]
```

```python
from contextlib import ExitStack

import concourse.bass as bass
from concourse import mybir

P = 128
F32 = mybir.dt.float32
F32R = mybir.dt.float32r
I32 = mybir.dt.int32
U32 = mybir.dt.uint32
ALU = mybir.AluOpType
ACT = mybir.ActivationFunctionType

CH = 256
BATCH = 64
CUTS = (0, 4, 7, 10, 13)
XPOS = 1
PACE = 0.9
XPOS = 1
PACE = 0.9
AHEAD = 10


def dlrm(nc, x, cat, emb, bw, bb, tw, tb, out):
    S, ND = x.shape
    T, V, E = emb.shape
    F = T + 1
    NCH, NB = S // CH, S // BATCH
    G = CH // 4
    GPB = BATCH * T // P
    STEPS = CH // 16
    NI = S * T // P
    IR = NI // 4
    D0, D1, D2 = (w.shape[1] for w in bw)
    H0, H1, H2, H3, _ = (w.shape[1] for w in tw)
    KX = tw[0].shape[0]
    XK = [min(P, KX - k * P) for k in range((KX + P - 1) // P)]
    assert E == P and D2 == P and GPB == CUTS[-1] and GPB * P == BATCH * T
    assert (26 * IR) % 26 == 0 and (P * IR) % T == 0

    with ExitStack() as ctx:
        def sb(name, shape, dt=F32):
            return ctx.enter_context(nc.sbuf_tensor(name, shape, dt))

        def psum(name, shape):
            return ctx.enter_context(nc.psum_tensor(name, shape, F32))

        def sem(name):
            return ctx.enter_context(nc.semaphore(name))

        unit = 512
        NU = (4 * H0 + 8 * H1 + 8 * H2 + 4 * H3) // unit
        w_hi = sb("w_hi", [P, NU * unit], F32R)
        w_lo = sb("w_lo", [P, NU * unit], F32R)
        w_last = sb("w_last", [P, 2])
        base = [0, 4 * H0, 4 * H0 + 8 * H1, 4 * H0 + 8 * H1 + 8 * H2]
        b_bot = sb("b_bot", [P, (D0 + D1 + D2) // P])
        b_top = sb("b_top", [P, (H0 + H1 + H2 + H3) // P])
        b_last = sb("b_last", [1, 1])
        ident = sb("ident", [P, P])
        idx = sb("idx", [P, NI], I32)
        idx_now = sb("idx_now", [P, 2, GPB], I32)
        offs = sb("offs", [P, GPB])
        offs_t = sb("offs_t", [P, GPB])
        bottom = sb("bottom", [P, S])
        rows = sb("rows", [P, GPB, E])
        feat = sb("feat", [P, BATCH, 32])
        gram = sb("gram", [P, F, G])
        act_f = sb("act_f", [P, 2, CH])
        stage = sb("stage", [P, 2, unit])
        ybuf = sb("ybuf", [1, CH])
        with nc.sbuf_tensor("early", [P, 7936], F32) as early:
            xT = early[:, 0:S]
            wb0 = early[0:16, S:S + D0]
            wb1 = early[:, S + 512:S + 1536].rearrange("p (k n) -> p k n", k=4)
            wb2 = early[:, S + 1536:S + 1792].rearrange("p (k n) -> p k n", k=2)
            x1 = early[:, S + 1792:S + 2816].rearrange("p (t n) -> p t n", t=4)
            x2 = early[:, S + 2816:S + 3328].rearrange("p (t n) -> p t n", t=2)
            slots = [stage[:, 0, :], stage[:, 1, :], act_f[:].rearrange("p a n -> p (a n)")] + \
                [early[:, S + 3328 + k * unit:S + 3328 + (k + 1) * unit] for k in range(5)]
        arena = sb("arena", [P, 6144], F32R)
        xin = sb("xin", [P, 2, 4, CH], F32R)
        h0 = arena[:, 0:4096].rearrange("p (a t n) -> p a t n", a=2, t=8)
        h1 = arena[:, 4096:6144].rearrange("p (a t n) -> p a t n", a=2, t=4)
        h2 = h0[:, :, 4:8]
        h3 = stage[:, 0, :].rearrange("p (t n) -> p t n", t=2)
        rows_flat = rows[:].rearrange("p i e -> p (i e)")
        cat_i = rows_flat[0:IR, 0:512].bitcast(I32)
        cat_f = rows_flat[0:IR, 512:1024]
        cat_w = rows_flat[0:IR, 1024:1536]
        gram_flat = gram[:].rearrange("p f g -> p (f g)")
        x_raw = gram_flat[:, 0:16 * ND].rearrange("p (b d) -> p b d", d=ND)

        Z = nc.dram_tensor("gram_scratch", (P, F, G), F32, kind="Internal").ap()
        Zv = Z.rearrange("(j m) f g -> m f j g", j=4)

        ps_t = psum("ps_t", [P, 2, 512])
        ps_g = psum("ps_g", [P, 2, 512])
        ps_m = psum("ps_m", [P, 2, 512])
        ps_a = psum("ps_a", [P, 2, 512])

        const_done = sem("const_done")
        zero_done = sem("zero_done")
        cat_in = sem("cat_in")
        x_loaded = sem("x_loaded")
        wb_in = sem("wb_in")
        bias_in = sem("bias_in")
        cat_step = sem("cat_step")
        offs_step = sem("offs_step")
        idx_turned = sem("idx_turned")
        idx_ready = sem("idx_ready")
        idx_copied = sem("idx_copied")
        steps_begun = sem("steps_begun")
        tiles_begun = sem("tiles_begun")
        x_turned = sem("x_turned")
        xT_step = sem("xT_step")
        stage_in = [sem(f"stage_in{i}") for i in range(len(slots))]
        w_split = sem("w_split")
        w_high = sem("w_high")
        gathered = [sem(f"gathered{i}") for i in range(4)]
        rows_turned = sem("rows_turned")
        feat_ready = sem("feat_ready")
        gram_done = sem("gram_done")
        gram_out = sem("gram_out")
        z_written = sem("z_written")
        pairs_in = [sem(f"pairs_in{i}") for i in range(3)]
        x_high = sem("x_high")
        x_ready = sem("x_ready")
        bot_mm = sem("bot_mm")
        bot_ev = sem("bot_ev")
        mlp_mm = sem("mlp_mm")
        mlp_ev = sem("mlp_ev")
        h_high = sem("h_high")
        h_split = sem("h_split")
        l2_step = sem("l2_step")
        y_out = sem("y_out")

        PRE = 3
        OUTS = ([("L0", m) for m in range(PRE, 8)] + [("L1", m) for m in range(8)] +
                [("L2", m) for m in range(4)] + [("N0", m) for m in range(PRE)] +
                [("L3", m) for m in range(2)] + [("L4", 0)])
        NO = len(OUTS)
        SPLIT = [o for o in OUTS if o[0] in ("L0", "L1", "L2", "N0")]
        NS = len(SPLIT)
        MM = [o for o in OUTS if o[0] in ("L0", "L1", "N0", "L3")]
        NM = len(MM)
        assert NS % 2 == 0 and NM % 2 == 0

        def out_no(c, o):
            return PRE + c * NO + OUTS.index(o) + 1

        def split_no(c, o):
            return PRE + c * NS + SPLIT.index(o) + 1

        def half(o, of):
            return (PRE + of.index(o)) % 2

        def body_order():
            items = [(("L0", m), 1.28) for m in range(PRE, 8)]
            for m in range(8):
                items.append((("L1", m), 2.56))
                if m:
                    items.append((("A", m - 1), 1.28))
            items.append((("A", 7), 1.28))
            items.insert(-XPOS, (("X", 0), 0.0))
            items += [(("N0", m), 1.28) for m in range(PRE)]
            items += [(("L3", m), 1.28) for m in range(2)] + [(("L4", 0), 0.85)]
            whole = sum(t for _, t in items)
            order, at, n = [], 0.0, 0
            for o, t in items:
                while n < STEPS and at >= (n + 0.5) * PACE * whole / STEPS:
                    order.append(("prep", n))
                    n += 1
                order.append(o)
                at += t
            while n < STEPS:
                order.append(("prep", n))
                n += 1
            return order

        ORDER = body_order()
        LEFT = STEPS - AHEAD

        def body_items(last, preps):
            for o in ORDER:
                if last and o[0] in ("N0", "X"):
                    continue
                if o[0] == "prep" and o[1] > preps:
                    continue
                yield o

        LEAD = (range(0, 4), range(4, 5), range(5, 6), range(6, 7))

        def bottom_bank(i):
            return (ps_m, ps_a)[i // 2 % 2][:, i % 2, 0:CH]

        TAIL = []
        for n in range(AHEAD):
            TAIL.append(("prep", STEPS + n))
            if n % 2 == 0 and n < 6:
                TAIL.append(("bottom", 5 + n // 2))
        assert AHEAD >= 5

        READS = []
        row = 0
        for m in range(T):
            f = m + 1
            while f < F:
                k, p0 = divmod(row, P)
                take = min(F - f, P - p0)
                READS.append((k, p0, take, m, f))
                f += take
                row += take
        assert D2 + row + 1 == KX
        reads = [sum(r[0] == k for r in READS) for k in range(3)]


        block = ctx.enter_context(nc.Block())

        def jg(ap):
            return ap.rearrange("p (g j) -> p j g", j=4)

        @block.sync
        def _(sp):
            sp.dma_start(cat_i, cat.rearrange("s t -> (s t)").rearrange("(b a q) -> a b q", a=IR, q=P))\
                .then_inc(cat_in, 16)
            sp.dma_start(x_raw, x.rearrange("(p b) d -> p b d", b=16)).then_inc(x_loaded, 16)
            sp.dma_start(wb0, bw[0]).then_inc(wb_in, 16)
            sp.dma_start(wb1, bw[1].rearrange("(k p) n -> p k n", p=P)).then_inc(wb_in, 16)
            sp.dma_start(wb2, bw[2].rearrange("(k p) n -> p k n", p=P)).then_inc(wb_in, 16)
            ctx.enter_context(nc.allow_non_contiguous_dma(reason="biases and last weights, once"))
            col = 0
            for b in bb:
                n = b.shape[0] // P
                sp.dma_start(b_bot[:, col:col + n], b.rearrange("(k p) -> p k", p=P)).then_inc(bias_in, 16)
                col += n
            col = 0
            for b in tb[:4]:
                n = b.shape[0] // P
                sp.dma_start(b_top[:, col:col + n], b.rearrange("(k p) -> p k", p=P)).then_inc(bias_in, 16)
                col += n
            sp.dma_start(b_last[:], tb[4].rearrange("(a b) -> a b", a=1)).then_inc(bias_in, 16)
            sp.dma_start(w_last[:], tw[4].rearrange("(k p) n -> p (k n)", p=P)).then_inc(bias_in, 16)

            u = 0
            for w in tw[:4]:
                K, N = w.shape
                per = min(N, unit)
                step = unit // per
                for k in range(0, (K + P - 1) // P, step):
                    for n in range(0, N, per):
                        if u >= len(slots):
                            sp.wait_ge(w_split, u - len(slots) + 1)
                        rows_here = min(P, K - k * P)
                        src = w[k * P:k * P + step * rows_here, n:n + per].rearrange("(k p) n -> p k n", k=step)
                        dst = slots[u % len(slots)][0:rows_here].rearrange("p (k n) -> p k n", k=step)
                        sp.dma_start(dst, src).then_inc(stage_in[u % len(slots)], 16)
                        u += 1
            assert u == NU

            def relayout(c, first=False):
                sp.wait_ge(gram_out, (c + 1) * STEPS)
                if not first:
                    for k in range(3):
                        sp.wait_ge(pairs_in[k], c * reads[k] * 16)
                sp.dma_start(Z, gram[:]).then_inc(z_written, 16)
                if first:
                    sp.wait_ge(w_split, NU)
                else:
                    sp.wait_ge(mlp_mm, out_no(c - 1, ("L0", 7)))
                sp.wait_ge(z_written, (c + 1) * 16)
                for k, p0, n, m, f in READS:
                    dst = xin[p0:p0 + n, 1, 1 + k, :].bitcast(F32).rearrange("p (j g) -> p j g", j=4)
                    sp.dma_start(dst, Zv[m, f:f + n]).then_inc(pairs_in[k], 16)

            relayout(0, True)
            with sp.Fori(0, NCH - 1) as c:
                relayout(c + 1)
            sp.wait_ge(y_out, NCH * 16 + 16)

        @block.gpsimd
        def _(pool):
            nc.gpsimd.memset(xT[0:16], 0.0).then_inc(zero_done, 1)
            nc.gpsimd.iota(idx_now[:, 0, :], [[-2, GPB]], base=T, channel_multiplier=1).then_inc(const_done, 1)
            nc.gpsimd.memset(ident[:], 0.0).then_inc(zero_done, 1)
            pool.wait_ge(zero_done, 2)
            nc.gpsimd.affine_select(out=ident[:], in_=ident[:], compare_op=ALU.not_equal, fill=1.0, base=0,
                                    pattern=[[-1, P]], channel_multiplier=1).then_inc(const_done, 1)
            pool.wait_ge(const_done, 2)
            nc.gpsimd.memset(xin[64:96, 1, 3, :].bitcast(F32), 0.0).then_inc(zero_done, 1)
            pool.wait_ge(zero_done, 3)
            nc.gpsimd.memset(early[96:128, S + 3328 + 3 * unit:], 0.0).then_inc(zero_done, 1)
            pool.wait_ge(zero_done, 4)
            nc.gpsimd.memset(feat[:, :, F:], 0.0).then_inc(zero_done, 1)
            table = emb.rearrange("t v e -> (t v) e")
            pool.wait_ge(idx_ready, 1)

            def batch(b, side, first=False):
                nc.gpsimd.tensor_copy(idx_now[:, side, :], idx[:, bass.ds(b * GPB, GPB)]).then_inc(idx_copied, 1)
                pool.wait_ge(idx_copied, b + 1)
                for k in range(4):
                    if not first:
                        pool.wait_ge(rows_turned, (b - 1) * 4 + k + 1)
                    pool.sem_inc(steps_begun, 1)
                    for i in range(CUTS[k], CUTS[k + 1]):
                        nc.gpsimd.indirect_dma_start(
                            rows[:, i, :], None, table,
                            bass.IndirectOffsetOnAxis(ap=idx_now[:, side, i:i + 1].bitcast(U32), axis=0),
                        ).then_inc(gathered[k], 16)

            batch(0, 0, True)
            batch(1, 1)
            with pool.Fori(1, NB // 2) as i:
                batch(i * 2, 0)
                batch(i * 2 + 1, 1)

        @block.scalar
        def _(act):
            def gram_quad(n, col, side):
                act.wait_ge(gram_done, n + 1)
                src = ps_g[:, side, 0:16 * F].rearrange("p (g j f) -> p j f g", g=4, j=4)
                for j in range(4):
                    a = 32 * j
                    last = nc.scalar.copy(gram[a:a + 32, :, bass.ds(col, 4)], src[a:a + 32, j])
                last.then_inc(gram_out, 1)

            xTv = xT[0:ND].rearrange("d (p b) -> d b p", b=16)
            act.wait_ge(zero_done, 1)
            for k in range(4):
                act.wait_ge(x_turned, k + 1)
                nc.scalar.copy(xTv[:, 4 * k:4 * k + 4, :],
                               (ps_t, ps_g)[k // 2][0:ND, k % 2, :].rearrange("d (b p) -> d b p", b=4))\
                    .then_inc(xT_step, 1)
            act.wait_ge(bias_in, 9 * 16)
            act.sem_inc(y_out, 16)

            def bottom_part(c, tiles):
                for i in tiles:
                    act.wait_ge(bot_mm, c * 7 + i + 1)
                    dst = x1[:, i, :] if i < 4 else x2[:, i - 4, :] if i < 6 else bottom[:, bass.ds(c * CH, CH)]
                    nc.scalar.activation(dst, bottom_bank(i), ACT.Relu,
                                         bias=b_bot[:, i:i + 1]).then_inc(bot_ev, 1)

            def lead(i, first=False):
                for k in range(4):
                    if not (first and k == 0):
                        gram_quad(i * 4 + k - 1, i * 16 + 4 * k - 4, (k - 1) % 2)
                    bottom_part(i + 1, LEAD[k])

            bottom_part(0, range(7))
            lead(0, True)
            with act.Fori(1, 4) as i:
                lead(i)
            for kind, n in TAIL:
                if kind == "bottom":
                    bottom_part(n, range(7))
                else:
                    if n == STEPS + 1:
                        act.wait_ge(z_written, 16)
                    gram_quad(n - 1, 4 * ((n - 1) % STEPS), (n - 1) % 2)

            def to_split(o, c, src, bias, no=None):
                if no is None:
                    act.wait_ge(h_split, split_no(c, o) - 2)
                    slot = half(o, SPLIT)
                else:
                    if no >= 2:
                        act.wait_ge(h_split, no - 1)
                    slot = no % 2
                nc.scalar.activation(act_f[:, slot, :], src, ACT.Relu, bias=b_top[:, bias:bias + 1])\
                    .then_inc(mlp_ev, 1)

            for m in range(PRE):
                act.wait_ge(mlp_mm, m + 1)
                to_split(None, 0, ps_m[:, m % 2, 0:CH], m, m)

            def body(c, last, preps):
                for o in body_items(last, preps):
                    kind, m = o
                    if kind == "prep":
                        q = (AHEAD + m - 1) % STEPS
                        if q == 0:
                            act.wait_ge(z_written, (c + 2) * 16)
                        gram_quad((c + 1) * STEPS + AHEAD + m - 1, 4 * q, q % 2)
                    elif kind in ("L0", "N0", "L1"):
                        act.wait_ge(mlp_mm, out_no(c, o))
                        to_split(o, c, ps_m[:, half(o, MM), 0:CH], m + (8 if kind == "L1" else 0))
                    elif o == ("A", 7):
                        for t in range(4):
                            act.wait_ge(mlp_mm, out_no(c, ("L2", t | 1)))
                            to_split(("L2", t), c, ps_a[:, t // 2, (t % 2) * CH:(t % 2 + 1) * CH], 16 + t)
                    elif kind == "L3":
                        act.wait_ge(mlp_mm, out_no(c, o) - 3 * last)
                        nc.scalar.activation(h3[:, m, :], ps_m[:, half(o, MM) ^ last, 0:CH], ACT.Relu,
                                             bias=b_top[:, 20 + m:21 + m]).then_inc(mlp_ev, 1)
                    elif kind == "L4":
                        act.wait_ge(mlp_mm, out_no(c, o) - 3 * last)
                        act.wait_ge(y_out, c * 16 + 16)
                        nc.scalar.activation(ybuf[0:1, :].rearrange("p (g j) -> p j g", j=4),
                                             ps_a[0:1, 0, 0:CH].rearrange("p (j g) -> p j g", j=4),
                                             ACT.Identity, bias=b_last[0:1, 0:1]).then_inc(mlp_ev, 1)
                        act.wait_ge(mlp_ev, out_no(c, o) - 3 * last)
                        act.dma_start(out[bass.ds(c * CH, CH), :].rearrange("s o -> o s"), ybuf[0:1, :])\
                            .then_inc(y_out, 16)

            with act.Fori(0, NCH - 2) as c:
                body(c, 0, STEPS)
            body(NCH - 2, 0, LEFT)
            body(NCH - 1, 1, -1)

        @block.vector
        def _(dve):
            dve.wait_ge(const_done, 1)
            nc.vector.tensor_copy(offs[:], idx_now[:, 0, :]).then_inc(offs_step, 1)
            step = 1
            for t in (4 * T, 2 * T, T):
                dve.wait_ge(offs_step, step)
                nc.vector.tensor_scalar(offs_t[:], offs[:], float(t), -float(t), ALU.is_ge, ALU.mult)\
                    .then_inc(offs_step, 1)
                dve.wait_ge(offs_step, step + 1)
                nc.vector.tensor_tensor(offs[:], offs[:], offs_t[:], ALU.add).then_inc(offs_step, 1)
                step += 2
            dve.wait_ge(offs_step, step)
            nc.vector.tensor_scalar(offs[:], offs[:], float(V), None, ALU.mult).then_inc(offs_step, 1)
            dve.wait_ge(cat_in, 16)
            nc.vector.tensor_scalar(cat_w, cat_i, 0.0, float(V), ALU.is_lt, ALU.mult).then_inc(cat_step, 1)
            dve.wait_ge(cat_step, 1)
            nc.vector.tensor_tensor(cat_f, cat_i, cat_w, ALU.add).then_inc(cat_step, 1)
            dve.wait_ge(cat_step, 2)
            nc.vector.tensor_scalar(cat_f, cat_f, 0.0, float(V - 1), ALU.max, ALU.min).then_inc(cat_step, 1)
            dve.wait_ge(idx_turned, 1)
            dve.wait_ge(offs_step, step + 1)
            nc.vector.tensor_tensor(idx[:].rearrange("p (c k) -> p c k", k=GPB),
                                    ps_m[:, 0, 0:NI].rearrange("p (c k) -> p c k", k=GPB),
                                    offs[:].unsqueeze(1).to_broadcast([P, NI // GPB, GPB]),
                                    ALU.add).then_inc(idx_ready, 1)
            def split(high, low, src, high_done, no, done):
                nc.vector.tensor_copy(high, src).then_inc(high_done, 1)
                dve.wait_ge(high_done, no)
                nc.vector.tensor_tensor(low, src, high.bitcast(F32), ALU.subtract).then_inc(done, 1)

            def weights(units):
                for u, s, turn in units:
                    dve.wait_ge(stage_in[s], turn * 16 + 16)
                    cols = bass.ds(u * unit, unit)
                    split(w_hi[:, cols], w_lo[:, cols], slots[s], w_high, u + 1, w_split)

            def features(n, b, k, first=False):
                at, end = P * CUTS[k], P * CUTS[k + 1]
                if not first:
                    dve.wait_ge(gram_done, n - 2)
                s0, s1 = -(-at // T), -(-end // T)
                cols = feat[:, :, 0:F]
                nc.vector.tensor_copy(cols[:, s0:s1, 0], bottom[:, bass.ds(b * BATCH + s0, s1 - s0)])
                dve.wait_ge(rows_turned, n + 1)
                src = ps_t[:, k % 2, 0:end - at]
                last = None
                if at % T:
                    m = T - at % T
                    nc.vector.tensor_copy(cols[:, s0 - 1, F - m:F], src[:, 0:m])
                whole = end // T - s0
                m = s0 * T - at
                last = nc.vector.tensor_copy(cols[:, s0:s0 + whole, 1:F],
                                             src[:, m:m + whole * T].rearrange("p (s f) -> p s f", f=T))
                m += whole * T
                if m < end - at:
                    last = nc.vector.tensor_copy(cols[:, s1 - 1, 1:1 + end - at - m], src[:, m:end - at])
                last.then_inc(feat_ready, 1)

            def lead(i, first=False):
                if first:
                    dve.wait_ge(bot_ev, 7)
                for k in range(4):
                    features(i * 4 + k, i, k, first)
                    weights([(i * 8 + s, s, i) for s in (2 * k, 2 * k + 1)])

            dve.wait_ge(zero_done, 4)
            lead(0, True)
            with dve.Fori(1, 4) as i:
                lead(i)
            weights([(u, u % 8, u // 8) for u in range(32, NU)])
            dve.wait_ge(bot_ev, 14)
            for n in range(STEPS, STEPS + AHEAD):
                features(n, n // 4, n % 4)

            def layer_input(c, first=False):
                if first:
                    dve.wait_ge(bot_ev, 7 * NCH)
                else:
                    dve.wait_ge(mlp_mm, out_no(c - 1, ("L0", 7)))
                view = lambda ap: ap.rearrange("p (j g) -> p j g", j=4)
                split(view(xin[:, 0, 0, :]), view(xin[:, 1, 0, :]),
                      bottom[:, bass.ds(c * CH, CH)].rearrange("p (g j) -> p j g", j=4),
                      x_high, c * 4 + 1, x_ready)
                for k in range(1, 4):
                    dve.wait_ge(pairs_in[k - 1], (c + 1) * (reads[k - 1] * 16))
                    rows_k = XK[k]
                    raw = xin[0:rows_k, 1, k, :]
                    nc.vector.tensor_copy(xin[0:rows_k, 0, k, :], raw.bitcast(F32)).then_inc(x_high, 1)
                    dve.wait_ge(x_high, c * 4 + k + 1)
                    nc.vector.tensor_tensor(raw, raw.bitcast(F32), xin[0:rows_k, 0, k, :].bitcast(F32),
                                            ALU.subtract).then_inc(x_ready, 1)

            def h_tile(dst, t, slot, no):
                dve.wait_ge(h_split_src[0], no[0])
                split(dst[:, 0, t, :], dst[:, 1, t, :], act_f[:, slot, :], h_high, no[1], h_split)

            h_split_src = [mlp_ev]
            layer_input(0, True)
            for m in range(PRE):
                h_tile(h0, m, m % 2, (m + 1, m + 1))

            def body(c, last, preps):
                for o in body_items(last, preps):
                    kind, m = o
                    if kind == "prep":
                        if m < preps:
                            features((c + 1) * STEPS + AHEAD + m, c * 4 + 4 + (AHEAD + m) // 4, (AHEAD + m) % 4)
                    elif kind == "X":
                        layer_input(c + 1)
                    elif kind in ("L0", "N0", "L1"):
                        h_tile(h1 if kind == "L1" else h0, m % 4 if kind == "L1" else m, half(o, SPLIT),
                               (out_no(c, o), split_no(c, o)))
                    elif o == ("A", 7):
                        for t in range(4):
                            o2 = ("L2", t)
                            h_tile(h2, t, half(o2, SPLIT), (out_no(c, o2), split_no(c, o2)))

            with dve.Fori(0, NCH - 2) as c:
                body(c, 0, STEPS)
            body(NCH - 2, 0, LEFT)
            body(NCH - 1, 1, -1)

        @block.tensor
        def _(pe):
            pe.wait_ge(const_done, 2)
            pe.wait_ge(cat_step, 3)
            for b in range(4):
                last = nc.tensor.transpose(ps_m[:, 0, b * IR:(b + 1) * IR], cat_f[:, b * P:(b + 1) * P],
                                           ident[0:IR, 0:IR])
            last.then_inc(idx_turned, 1)
            pe.wait_ge(x_loaded, 16)
            for k in range(4):
                ps = (ps_t, ps_g)[k // 2]
                for b in range(4):
                    last = nc.tensor.transpose(ps[0:ND, k % 2, b * P:(b + 1) * P], x_raw[:, 4 * k + b, :],
                                               ident[:])
                last.then_inc(x_turned, 1)

            def product(acc, whi, wlo, xhi, xlo, start, stop, shared=False):
                nc.tensor.matmul(acc, whi, xhi, start=start, stop=False, skip_group_check=shared)
                nc.tensor.matmul(acc, whi, xlo, start=False, stop=False, skip_group_check=shared)
                return nc.tensor.matmul(acc, wlo, xhi, start=False, stop=stop, skip_group_check=shared)

            def bottom_part(c, tiles, first=False):
                for i in tiles:
                    if i < 4:
                        if i == 0 and not first:
                            pe.wait_ge(bot_ev, c * 7)
                        pe.sem_inc(tiles_begun, 1)
                        last = nc.tensor.matmul(bottom_bank(i), wb0[:, i * P:(i + 1) * P],
                                                xT[0:16, bass.ds(c * CH, CH)], start=True, stop=True)
                    elif i < 6:
                        for k in range(4):
                            pe.wait_ge(bot_ev, c * 7 + (k + 1 if i == 4 else 4))
                            last = nc.tensor.matmul(bottom_bank(i), wb1[:, k, (i - 4) * P:(i - 3) * P], x1[:, k, :],
                                                    start=k == 0, stop=k == 3)
                    else:
                        for k in range(2):
                            pe.wait_ge(bot_ev, c * 7 + 5 + k)
                            last = nc.tensor.matmul(bottom_bank(i), wb2[:, k, :], x2[:, k, :],
                                                    start=k == 0, stop=k == 1)
                    last.then_inc(bot_mm, 1)

            def turn(n, b, k, first=False):
                if not first:
                    pe.wait_ge(feat_ready, n - 1)
                pe.wait_ge(gathered[k], (b + 1) * (16 * (CUTS[k + 1] - CUTS[k])))
                for i in range(CUTS[k], CUTS[k + 1]):
                    a = P * (i - CUTS[k])
                    last = nc.tensor.transpose(ps_t[:, k % 2, a:a + P], rows[:, i, :], ident[:])
                last.then_inc(rows_turned, 1)

            def gram_products(n, k, first=False):
                pe.wait_ge(feat_ready, n + 1)
                if not first:
                    pe.wait_ge(gram_out, n - 1)
                for g in range(4):
                    four = feat[:, 16 * k + 4 * g:16 * k + 4 * g + 4, :]
                    last = nc.tensor.matmul(ps_g[:, k % 2, g * 4 * F:(g + 1) * 4 * F],
                                            four.rearrange("p s f -> p (s f)"), four[:, :, 0:F],
                                            start=True, stop=True)
                last.then_inc(gram_done, 1)

            pe.wait_ge(wb_in, 3 * 16)
            pe.wait_ge(xT_step, 4)
            pe.wait_ge(idx_ready, 1)
            pe.wait_ge(zero_done, 5)

            def lead(i, first=False):
                for k in range(4):
                    if not (first and k == 0):
                        gram_products(i * 4 + k - 1, (k - 1) % 4, first and k < 3)
                    turn(i * 4 + k, i, k, first and k < 2)
                    bottom_part(i + 1, LEAD[k])

            bottom_part(0, range(7), True)
            lead(0, True)
            with pe.Fori(1, 4) as i:
                lead(i)
            for kind, n in TAIL:
                if kind == "bottom":
                    bottom_part(n, range(7))
                else:
                    gram_products(n - 1, (n - 1) % 4)
                    turn(n, n // 4, n % 4)

            def layer(acc, layer_no, N, m, tiles, x, ready=None):
                for k in range(tiles):
                    if ready is not None:
                        ready(k)
                    K = XK[k] if layer_no == 0 else P
                    cols = slice(base[layer_no] + k * N + m * P, base[layer_no] + k * N + (m + 1) * P)
                    last = product(acc, w_hi[0:K, cols], w_lo[0:K, cols], x[0:K, 0, k, :], x[0:K, 1, k, :],
                                   k == 0, k == tiles - 1)
                return last

            pe.wait_ge(w_split, NU)
            for m in range(PRE):
                if m >= 2:
                    pe.wait_ge(mlp_ev, m - 1)
                layer(ps_m[:, m % 2, 0:CH], 0, H0, m, 4, xin,
                      (lambda k: pe.wait_ge(x_ready, k + 1)) if m == 0 else None).then_inc(mlp_mm, 1)

            def body(c, last_body, preps):
                for o in body_items(last_body, preps):
                    kind, m = o
                    if kind in ("L0", "L1", "N0", "L3"):
                        j = MM.index(o) - 3 * (last_body and kind == "L3")
                        side = (PRE + j) % 2
                        acc = ps_m[:, side, 0:CH]
                        pe.wait_ge(mlp_ev, out_no(c, MM[j - 2]) if j >= 2 else out_no(c - 1, OUTS[j - 2]))
                    if kind == "prep":
                        n = (c + 1) * STEPS + AHEAD + m
                        k = (AHEAD + m) % 4
                        gram_products(n - 1, (k - 1) % 4)
                        if m < preps:
                            turn(n, c * 4 + 4 + (AHEAD + m) // 4, k)
                    elif kind == "L0":
                        layer(acc, 0, H0, m, 4, xin).then_inc(mlp_mm, 1)
                    elif kind == "N0":
                        layer(acc, 0, H0, m, 4, xin,
                              (lambda k: pe.wait_ge(x_ready, (c + 1) * 4 + k + 1)) if m == 0 else None)\
                            .then_inc(mlp_mm, 1)
                    elif kind == "L1":
                        def h0_ready(k):
                            if k == 0:
                                pe.wait_ge(h_split, split_no(c, ("L0", PRE)) - 1)
                            elif k >= PRE:
                                pe.wait_ge(h_split, split_no(c, ("L0", k)))
                        layer(acc, 1, H1, m, 8, h0, h0_ready if m == 0 else None).then_inc(mlp_mm, 1)
                    elif kind == "A":
                        if m == 0:
                            pe.wait_ge(mlp_ev, out_no(c - 1, ("L4", 0)))
                        pe.wait_ge(h_split, split_no(c, ("L1", m)))
                        for t in range(4):
                            cols = slice(base[2] + m * H2 + t * P, base[2] + m * H2 + (t + 1) * P)
                            last = product(ps_a[:, t // 2, (t % 2) * CH:(t % 2 + 1) * CH], w_hi[:, cols],
                                           w_lo[:, cols], h1[:, 0, m % 4, :], h1[:, 1, m % 4, :],
                                           m == 0 and t % 2 == 0, m == 7, shared=True)
                            if m == 7:
                                last.then_inc(mlp_mm, 1)
                    elif kind == "L3":
                        layer(acc, 3, H3, m, 4, h2,
                              (lambda k: pe.wait_ge(h_split, split_no(c, ("L2", k)))) if m == 0 else None)\
                            .then_inc(mlp_mm, 1)
                    elif kind == "L4":
                        pe.wait_ge(mlp_ev, out_no(c, ("L3", 1)) - 3 * last_body)
                        for k in range(2):
                            last = nc.tensor.matmul(ps_a[0:1, 0, 0:CH], w_last[:, k:k + 1], h3[:, k, :],
                                                    start=k == 0, stop=k == 1)
                        last.then_inc(mlp_mm, 1)

            with pe.Fori(0, NCH - 2) as c:
                body(c, 0, STEPS)
            body(NCH - 2, 0, LEFT)
            body(NCH - 1, 1, -1)


_INS = ["r_numerical", "r_cat_features", "L0_rec_emb_tables"] + \
    [f"L0_rec_b{p}{i}" for p in "wb" for i in range(3)] + [f"L0_rec_t{p}{i}" for p in "wb" for i in range(5)]


def kernel(**inputs):
    import numpy as np
    import concourse.bacc as bacc
    from concourse.bass_utils import run_bass_kernel_spmd as run

    nc = bacc.Bacc("TRN2", target_bir_lowering=False, num_devices=1)
    arrays, aps = {}, []
    for name in _INS:
        a = np.ascontiguousarray(inputs[name])
        arrays[f"in_{name}"] = a
        aps.append(nc.dram_tensor(f"in_{name}", a.shape, mybir.dt.from_np(a.dtype), kind="ExternalInput").ap())
    x, cat, emb = aps[:3]
    out = nc.dram_tensor("out_y", (x.shape[0], 1), F32, kind="ExternalOutput").ap()
    dlrm(nc, x, cat, emb, aps[3:6], aps[6:9], aps[9:14], aps[14:19], out)
    return run(nc, [arrays], core_ids=[0]).results[0]["out_y"]
```
